# Optimizing a Trainium2 kernel written in Bass

```python
import numpy as np
import jax
import jax.numpy as jnp

def _softmax(x, axis=-1):
    return jax.nn.softmax(x, axis=axis)

def _gelu(x):
    return jax.nn.gelu(x, approximate=True)

def _silu(x):
    return jax.nn.silu(x)

def _sigmoid(x):
    return jax.nn.sigmoid(x)

def _layernorm(x, axis=-1, eps=1e-05):
    m = jnp.mean(x, axis=axis, keepdims=True)
    v = jnp.var(x, axis=axis, keepdims=True)
    return (x - m) / jnp.sqrt(v + eps)

def _scatter_add(tgt, idx, src, axis=0):
    return tgt.at[idx].add(src)

def _segment_sum(src, seg, n):
    return jax.ops.segment_sum(src, seg, n)
kernel_name = 'mk_dlrm_tower_d1_rec_r8_bb2b1b'

def setup_inputs(seed: int=0):
    np.random.seed(seed)
    _w = jnp.asarray

    def _rec_inputs():
        import jax
        import jax.numpy as jnp
        _tk = jax.random.key(seed)
        ids = jnp.stack([jax.random.randint(jax.random.fold_in(_tk, 200 + f), (2048,), 0, v, jnp.int32) for f, v in enumerate([12500, 1250, 12500, 125000, 1250, 12500, 1000, 12500, 1000, 12500, 12500, 1000, 1250, 12500, 1250, 12500, 1250, 1250, 1000, 1250, 1250, 1000, 1000, 1000, 1250, 1250])], axis=1)
        tbl_0 = 0.05 * jax.random.normal(jax.random.fold_in(_tk, 500 + 0), (12500, 128), jnp.float32)
        tbl_1 = 0.05 * jax.random.normal(jax.random.fold_in(_tk, 500 + 1), (1250, 128), jnp.float32)
        tbl_2 = 0.05 * jax.random.normal(jax.random.fold_in(_tk, 500 + 2), (12500, 128), jnp.float32)
        tbl_3 = 0.05 * jax.random.normal(jax.random.fold_in(_tk, 500 + 3), (125000, 128), jnp.float32)
        tbl_4 = 0.05 * jax.random.normal(jax.random.fold_in(_tk, 500 + 4), (1250, 128), jnp.float32)
        tbl_5 = 0.05 * jax.random.normal(jax.random.fold_in(_tk, 500 + 5), (12500, 128), jnp.float32)
        tbl_6 = 0.05 * jax.random.normal(jax.random.fold_in(_tk, 500 + 6), (1000, 128), jnp.float32)
        tbl_7 = 0.05 * jax.random.normal(jax.random.fold_in(_tk, 500 + 7), (12500, 128), jnp.float32)
        tbl_8 = 0.05 * jax.random.normal(jax.random.fold_in(_tk, 500 + 8), (1000, 128), jnp.float32)
        tbl_9 = 0.05 * jax.random.normal(jax.random.fold_in(_tk, 500 + 9), (12500, 128), jnp.float32)
        tbl_10 = 0.05 * jax.random.normal(jax.random.fold_in(_tk, 500 + 10), (12500, 128), jnp.float32)
        tbl_11 = 0.05 * jax.random.normal(jax.random.fold_in(_tk, 500 + 11), (1000, 128), jnp.float32)
        tbl_12 = 0.05 * jax.random.normal(jax.random.fold_in(_tk, 500 + 12), (1250, 128), jnp.float32)
        tbl_13 = 0.05 * jax.random.normal(jax.random.fold_in(_tk, 500 + 13), (12500, 128), jnp.float32)
        tbl_14 = 0.05 * jax.random.normal(jax.random.fold_in(_tk, 500 + 14), (1250, 128), jnp.float32)
        tbl_15 = 0.05 * jax.random.normal(jax.random.fold_in(_tk, 500 + 15), (12500, 128), jnp.float32)
        tbl_16 = 0.05 * jax.random.normal(jax.random.fold_in(_tk, 500 + 16), (1250, 128), jnp.float32)
        tbl_17 = 0.05 * jax.random.normal(jax.random.fold_in(_tk, 500 + 17), (1250, 128), jnp.float32)
        tbl_18 = 0.05 * jax.random.normal(jax.random.fold_in(_tk, 500 + 18), (1000, 128), jnp.float32)
        tbl_19 = 0.05 * jax.random.normal(jax.random.fold_in(_tk, 500 + 19), (1250, 128), jnp.float32)
        tbl_20 = 0.05 * jax.random.normal(jax.random.fold_in(_tk, 500 + 20), (1250, 128), jnp.float32)
        tbl_21 = 0.05 * jax.random.normal(jax.random.fold_in(_tk, 500 + 21), (1000, 128), jnp.float32)
        tbl_22 = 0.05 * jax.random.normal(jax.random.fold_in(_tk, 500 + 22), (1000, 128), jnp.float32)
        tbl_23 = 0.05 * jax.random.normal(jax.random.fold_in(_tk, 500 + 23), (1000, 128), jnp.float32)
        tbl_24 = 0.05 * jax.random.normal(jax.random.fold_in(_tk, 500 + 24), (1250, 128), jnp.float32)
        tbl_25 = 0.05 * jax.random.normal(jax.random.fold_in(_tk, 500 + 25), (1250, 128), jnp.float32)
        _rk = jax.random.fold_in(_tk, 7)
        r_dense_x = -0.000514642 + 1.00011 * jax.random.normal(jax.random.fold_in(_rk, 101), (2048, 128), jnp.float32)
        W_top1 = 0.0456912 * jax.random.normal(jax.random.fold_in(_tk, 801), (479, 512), jnp.float32)
        W_top2 = 0.0441942 * jax.random.normal(jax.random.fold_in(_tk, 802), (512, 256), jnp.float32)
        W_top3 = 0.0625 * jax.random.normal(jax.random.fold_in(_tk, 803), (256, 1), jnp.float32)
        b_top1 = jnp.zeros((512,), jnp.float32)
        b_top2 = jnp.zeros((256,), jnp.float32)
        return (r_dense_x, ids, tbl_0, tbl_1, tbl_2, tbl_3, tbl_4, tbl_5, tbl_6, tbl_7, tbl_8, tbl_9, tbl_10, tbl_11, tbl_12, tbl_13, tbl_14, tbl_15, tbl_16, tbl_17, tbl_18, tbl_19, tbl_20, tbl_21, tbl_22, tbl_23, tbl_24, tbl_25, W_top1, b_top1, W_top2, b_top2, W_top3)
    r_dense_x, ids, tbl_0, tbl_1, tbl_2, tbl_3, tbl_4, tbl_5, tbl_6, tbl_7, tbl_8, tbl_9, tbl_10, tbl_11, tbl_12, tbl_13, tbl_14, tbl_15, tbl_16, tbl_17, tbl_18, tbl_19, tbl_20, tbl_21, tbl_22, tbl_23, tbl_24, tbl_25, W_top1, b_top1, W_top2, b_top2, W_top3 = _rec_inputs()

    def _L0_rec_setup():
        import jax, jax.numpy as jnp
        import numpy as np
        F = 26
        D = 128
        B = 2048
        _TRIU_I, _TRIU_J = np.triu_indices(F + 1, k=1)
        _TRIU_I = jnp.asarray(_TRIU_I)
        _TRIU_J = jnp.asarray(_TRIU_J)
        key = jax.random.key(seed)
        k1, k2 = jax.random.split(key)
        sparse_x = jax.random.normal(k1, (B, F, D), dtype=jnp.float32)
        dense_x = jax.random.normal(k2, (B, D), dtype=jnp.float32)
        return {'sparse_x': sparse_x, 'dense_x': dense_x}
    _L0_rec_all = _L0_rec_setup()
    _L0_rec_in = {k: v for k, v in _L0_rec_all.items() if k in ()}
    del _L0_rec_all
    return {'r_dense_x': r_dense_x, 'ids': ids, 'tbl_0': tbl_0, 'tbl_1': tbl_1, 'tbl_2': tbl_2, 'tbl_3': tbl_3, 'tbl_4': tbl_4, 'tbl_5': tbl_5, 'tbl_6': tbl_6, 'tbl_7': tbl_7, 'tbl_8': tbl_8, 'tbl_9': tbl_9, 'tbl_10': tbl_10, 'tbl_11': tbl_11, 'tbl_12': tbl_12, 'tbl_13': tbl_13, 'tbl_14': tbl_14, 'tbl_15': tbl_15, 'tbl_16': tbl_16, 'tbl_17': tbl_17, 'tbl_18': tbl_18, 'tbl_19': tbl_19, 'tbl_20': tbl_20, 'tbl_21': tbl_21, 'tbl_22': tbl_22, 'tbl_23': tbl_23, 'tbl_24': tbl_24, 'tbl_25': tbl_25, 'W_top1': W_top1, 'b_top1': b_top1, 'W_top2': W_top2, 'b_top2': b_top2, 'W_top3': W_top3}

def reference(r_dense_x, ids, tbl_0, tbl_1, tbl_2, tbl_3, tbl_4, tbl_5, tbl_6, tbl_7, tbl_8, tbl_9, tbl_10, tbl_11, tbl_12, tbl_13, tbl_14, tbl_15, tbl_16, tbl_17, tbl_18, tbl_19, tbl_20, tbl_21, tbl_22, tbl_23, tbl_24, tbl_25, W_top1, b_top1, W_top2, b_top2, W_top3):
    import jax
    import jax.numpy as jnp

    def _L0_rec_ref(sparse_x, dense_x):
        import jax, jax.numpy as jnp
        import numpy as np
        F = 26
        D = 128
        B = 2048
        _TRIU_I, _TRIU_J = np.triu_indices(F + 1, k=1)
        _TRIU_I = jnp.asarray(_TRIU_I)
        _TRIU_J = jnp.asarray(_TRIU_J)
        combined = jnp.concatenate([sparse_x, dense_x[:, None, :]], axis=1)
        interact = jnp.einsum('bfd,bgd->bfg', combined, combined)
        return interact[:, _TRIU_I, _TRIU_J]
    e = jnp.stack([tbl_0[ids[:, 0]], tbl_1[ids[:, 1]], tbl_2[ids[:, 2]], tbl_3[ids[:, 3]], tbl_4[ids[:, 4]], tbl_5[ids[:, 5]], tbl_6[ids[:, 6]], tbl_7[ids[:, 7]], tbl_8[ids[:, 8]], tbl_9[ids[:, 9]], tbl_10[ids[:, 10]], tbl_11[ids[:, 11]], tbl_12[ids[:, 12]], tbl_13[ids[:, 13]], tbl_14[ids[:, 14]], tbl_15[ids[:, 15]], tbl_16[ids[:, 16]], tbl_17[ids[:, 17]], tbl_18[ids[:, 18]], tbl_19[ids[:, 19]], tbl_20[ids[:, 20]], tbl_21[ids[:, 21]], tbl_22[ids[:, 22]], tbl_23[ids[:, 23]], tbl_24[ids[:, 24]], tbl_25[ids[:, 25]]], axis=1)
    z = _L0_rec_ref(e, r_dense_x)
    z = z.reshape(z.shape[0], -1)
    h = jnp.concatenate([z, r_dense_x], axis=1)
    h = jnp.maximum(h @ W_top1 + b_top1, 0.0)
    h = jnp.maximum(h @ W_top2 + b_top2, 0.0)
    y = h @ W_top3
    return y

_drawn_inputs = setup_inputs


def setup_inputs(seed=0):
    import zlib

    import numpy as np

    out = dict(_drawn_inputs(seed))
    spreads = {'b_top1': (0.0, 0.1), 'b_top2': (0.0, 0.1)}
    factors = {}
    for name, (base, spread) in spreads.items():
        noise = np.random.default_rng([zlib.crc32(name.encode()), seed]).standard_normal(out[name].shape)
        drawn = base * np.exp(spread * noise) if base else spread * noise
        out[name] = jnp.asarray(drawn.astype(out[name].dtype))
    for name, factor in factors.items():
        out[name] = (out[name] * factor).astype(out[name].dtype)
    return out
```

```python
from contextlib import ExitStack

import concourse.bass as bass
from concourse import mybir

F32 = mybir.dt.float32
I32 = mybir.dt.int32
ALU = mybir.AluOpType
ACT = mybir.ActivationFunctionType

P = 128
DMA = 16
TILES_PER_TURN = 2
GROUP = 4
QUADS = 4


def dlrm_tower(nc, x_t, ids, tables, w1, b1, w2, b2, w3, y_out):
    B, F = ids.shape
    D = x_t.shape[0]
    NF = F + 1
    H1, H2 = w1.shape[1], w2.shape[1]
    N1, N2 = H1 // P, H2 // P
    TILES = B // P
    TURNS = TILES // TILES_PER_TURN
    HALF = 2 * P
    GROUPS = [list(range(f, min(f + GROUP, F))) for f in range(0, F, GROUP)]
    NG = len(GROUPS)
    BANK_SAMPLES = P // 2
    ROUNDS = BANK_SAMPLES // QUADS
    assert D == P and TILES % TILES_PER_TURN == 0 and NG % 2 == 1
    assert ROUNDS * F * 4 <= 2048

    pair_row = [sum(F - r for r in range(i)) for i in range(F)]
    PAIRS = F * NF // 2
    k_rows = [min(P, PAIRS - k) for k in range(0, PAIRS, P)]
    KZ = len(k_rows)
    z_moves = []
    for i in range(F):
        at, j, end = pair_row[i], i, F
        while j < end:
            n = min(end - j, P - at % P)
            z_moves.append((i, j, n, at // P, at % P))
            at, j = at + n, j + n

    with ExitStack() as ctx:
        def sb(name, shape, dt=F32):
            return ctx.enter_context(nc.sbuf_tensor(name, shape, dt))

        def psum(name, shape):
            return ctx.enter_context(nc.psum_tensor(name, shape, F32))

        def sem(name):
            return ctx.enter_context(nc.semaphore(name))

        identity = sb("identity", [P, P])
        x_sb = sb("x_sb", [P, B])
        idx_all = sb("idx_all", [P, TILES, F], I32)
        idx = sb("idx", [P, TILES_PER_TURN, F], I32)
        rows = sb("rows", [P, TILES_PER_TURN, F, D])
        emb = sb("emb", [P, TILES_PER_TURN, P, NF])
        dots = sb("dots", [F, F, HALF])
        z = sb("z", [P, KZ, HALF])
        w1_sb = sb("w1_sb", [P, KZ + 1, H1])
        w2_sb = sb("w2_sb", [P, N1, H2])
        w3_sb = sb("w3_sb", [P, N2])
        b1_sb = sb("b1_sb", [P, N1])
        b2_sb = sb("b2_sb", [P, N2])
        h1 = sb("h1", [P, N1, HALF])
        h2 = sb("h2", [P, N2, HALF])
        y_sb = sb("y_sb", [1, B])

        turned = [psum(f"turned{i}", [P, 512]) for i in range(2)]
        dot_ps = [psum(f"dot_ps{i}", [P, 512]) for i in range(2)]
        h1_ps = psum("h1_ps", [P, N1, HALF])
        h2_ps = psum("h2_ps", [P, N2, HALF])
        y_ps = psum("y_ps", [P, 512])

        weights_in = sem("weights_in")
        x_in = sem("x_in")
        identity_zero = sem("identity_zero")
        identity_ready = sem("identity_ready")
        idx_in = sem("idx_in")
        idx_ready = sem("idx_ready")
        rows_in = [[sem(f"rows_in{u}_{g}") for g in range(NG)] for u in range(TILES_PER_TURN)]
        pool_steps = sem("pool_steps")
        sp_steps = sem("sp_steps")
        turned_full = sem("turned_full")
        emb_act = sem("emb_act")
        emb_dve = sem("emb_dve")
        emb_x = sem("emb_x")
        dots_full = [sem(f"dots_full{k}") for k in range(2)]
        dots_act = sem("dots_act")
        dots_dve = sem("dots_dve")
        z_in = sem("z_in")
        h1_full = sem("h1_full")
        h1_ready = sem("h1_ready")
        h2_full = sem("h2_full")
        h2_ready = sem("h2_ready")
        y_full = sem("y_full")
        y_ready = sem("y_ready")
        y_stored = sem("y_stored")

        def count(value):
            return not isinstance(value, int) or value > 0

        def tiles_before(turn, u):
            return turn * TILES_PER_TURN + u

        def groups_before(turn, u, g):
            return turn * (TILES_PER_TURN * NG) + (u * NG + g)

        def even_groups_before(turn, u, g):
            return turn * (TILES_PER_TURN * NG // 2) + (u * NG + g + 1) // 2

        def odd_groups_before(turn, u, g):
            return turn * (TILES_PER_TURN * NG // 2) + (u * NG + g) // 2

        def is_even(u, g):
            return (u * NG + g) % 2 == 0

        block = ctx.enter_context(nc.Block())

        @block.sync
        def _(sp):
            def move_pairs(half):
                sp.wait_ge(dots_act, half * 2 + 2)
                sp.wait_ge(dots_dve, half * 2 + 2)
                sp.sem_inc(sp_steps, 1)
                if count(half):
                    sp.wait_ge(h1_full, half * N1)
                for i, j, n, chunk, row in z_moves:
                    sp.dma_start(z[row:row + n, chunk, :], dots[i:i + 1, j:j + n, :]).then_inc(z_in, DMA)

            sp.dma_start(idx_all[:, :, :], ids.rearrange("(t p) f -> p t f", p=P)).then_inc(idx_in, DMA)
            sp.dma_start(x_sb[:, :], x_t).then_inc(x_in, DMA)
            for c, k in enumerate(k_rows):
                sp.dma_start(w1_sb[0:k, c, :], w1[c * P:c * P + k, :]).then_inc(weights_in, DMA)
            sp.dma_start(w1_sb[:, KZ, :], w1[PAIRS:PAIRS + D, :]).then_inc(weights_in, DMA)
            sp.dma_start(w2_sb[:, :, :], w2.rearrange("(c p) n -> p c n", p=P)).then_inc(weights_in, DMA)
            sp.dma_start(w3_sb[:, :], w3).then_inc(weights_in, DMA)
            sp.dma_start(b1_sb[:, :], b1).then_inc(weights_in, DMA)
            sp.dma_start(b2_sb[:, :], b2).then_inc(weights_in, DMA)
            move_pairs(0)
            with sp.Fori(1, TURNS) as turn:
                move_pairs(turn)
            sp.wait_ge(y_ready, B // HALF)
            sp.dma_start(y_out, y_sb[:, :]).then_inc(y_stored, DMA)
            sp.wait_ge(y_stored, DMA)

        WEIGHTS = DMA * (KZ + 1 + 4)

        @block.gpsimd
        def _(pool):
            pool.memset(identity[:, :], 0.0).then_inc(identity_zero, 1)
            pool.wait_ge(identity_zero, 1)
            pool.affine_select(out=identity[:, :], in_=identity[:, :], compare_op=ALU.not_equal, fill=1.0,
                               base=0, pattern=[[-1, P]], channel_multiplier=1).then_inc(identity_ready, 1)

            def gather(turn, u):
                if count(turn):
                    pool.wait_ge(turned_full, groups_before(turn - 1, u, NG))
                    pool.sem_inc(pool_steps, 1)
                pool.tensor_copy(idx[:, u, :], idx_all[:, tiles_before(turn, u), :]).then_inc(idx_ready, 1)
                for g, group in enumerate(GROUPS):
                    if g == 0:
                        pool.wait_ge(idx_ready, tiles_before(turn, u) + 1)
                    if count(turn):
                        pool.wait_ge(turned_full, groups_before(turn - 1, u, g) + 1)
                    pool.sem_inc(pool_steps, 1)
                    for f in group:
                        pool.indirect_dma_start(
                            out=rows[:, u, f, :], out_offset=None, in_=tables[f],
                            in_offset=bass.IndirectOffsetOnAxis(ap=idx[:, u, f:f + 1], axis=0),
                        ).then_inc(rows_in[u][g], DMA)

            pool.wait_ge(idx_in, DMA)
            for u in range(TILES_PER_TURN):
                gather(0, u)
            with pool.Fori(1, TURNS) as turn:
                for u in range(TILES_PER_TURN):
                    gather(turn, u)

        @block.tensor
        def _(pe):
            def transpose_tile(turn, u):
                for g, group in enumerate(GROUPS):
                    pe.wait_ge(rows_in[u][g], turn * (DMA * len(group)) + DMA * len(group))
                    if is_even(u, g):
                        bank, taken, before = turned[0], emb_act, even_groups_before(turn, u, g)
                    else:
                        bank, taken, before = turned[1], emb_dve, odd_groups_before(turn, u, g)
                    if count(before):
                        pe.wait_ge(taken, before)
                    for n, f in enumerate(group):
                        last = pe.transpose(bank[:, n * P:(n + 1) * P], rows[:, u, f, :], identity[:, :])
                    last.then_inc(turned_full, 1)

            def dot_tile(turn, u):
                pe.wait_ge(emb_act, even_groups_before(turn, u, NG))
                pe.wait_ge(emb_dve, odd_groups_before(turn, u, NG))
                pe.wait_ge(emb_x, tiles_before(turn, u) + 1)
                for k, taken in enumerate((dots_act, dots_dve)):
                    before = tiles_before(turn, u)
                    if count(before):
                        pe.wait_ge(taken, before)
                    for r in range(ROUNDS):
                        for a in range(QUADS):
                            s = k * BANK_SAMPLES + r * QUADS + a
                            last = pe.matmul(dot_ps[k][32 * a:32 * a + F, r * F:(r + 1) * F],
                                             emb[:, u, s, 0:F], emb[:, u, s, 1:NF], start=True, stop=True)
                    last.then_inc(dots_full[k], 1)

            def mlp(half):
                pe.wait_ge(z_in, half * (DMA * len(z_moves)) + DMA * len(z_moves))
                for n in range(N1):
                    for c, k in enumerate(k_rows):
                        pe.matmul(h1_ps[:, n, :], w1_sb[0:k, c, n * P:(n + 1) * P], z[0:k, c, :],
                                  start=c == 0, stop=False)
                    pe.matmul(h1_ps[:, n, :], w1_sb[:, KZ, n * P:(n + 1) * P],
                              x_sb[:, bass.ds(half * HALF, HALF)], start=False, stop=True).then_inc(h1_full, 1)
                for n in range(N2):
                    for c in range(N1):
                        if n == 0:
                            pe.wait_ge(h1_ready, half * N1 + c + 1)
                        last = pe.matmul(h2_ps[:, n, :], w2_sb[:, c, n * P:(n + 1) * P], h1[:, c, :],
                                         start=c == 0, stop=c == N1 - 1)
                    last.then_inc(h2_full, 1)
                for c in range(N2):
                    pe.wait_ge(h2_ready, half * N2 + c + 1)
                    last = pe.matmul(y_ps[0:1, 0:HALF], w3_sb[:, c:c + 1], h2[:, c, :],
                                     start=c == 0, stop=c == N2 - 1)
                last.then_inc(y_full, 1)

            pe.wait_ge(identity_ready, 1)
            for u in range(TILES_PER_TURN):
                transpose_tile(0, u)
                dot_tile(0, u)
            pe.wait_ge(weights_in, WEIGHTS)
            pe.wait_ge(x_in, DMA)
            with pe.Fori(1, TURNS) as turn:
                transpose_tile(turn, 0)
                dot_tile(turn, 0)
                mlp(turn - 1)
                transpose_tile(turn, 1)
                dot_tile(turn, 1)
            mlp(TURNS - 1)

        def copy_group(eng, copy, turn, u, g, done):
            eng.wait_ge(turned_full, groups_before(turn, u, g) + 1)
            if g < 2:
                if count(turn):
                    eng.wait_ge(dots_full[1], tiles_before(turn - 1, u) + 1)
            group = GROUPS[g]
            source = turned[0 if is_even(u, g) else 1][:, 0:len(group) * P].rearrange("d (f s) -> d f s", s=P)
            target = emb[:, u, :, group[0]:group[-1] + 1].rearrange("d s f -> d f s")
            copy(target, source).then_inc(done, 1)

        def copy_dots(eng, copy, turn, u, k, done):
            tile = tiles_before(turn, u)
            eng.wait_ge(dots_full[k], tile + 1)
            if u % 2 == 0 and count(turn):
                eng.wait_ge(z_in, turn * (DMA * len(z_moves)))
            first = (u % 2) * P + k * BANK_SAMPLES
            for a in range(QUADS):
                source = dot_ps[k][32 * a:32 * a + F, 0:ROUNDS * F].rearrange("i (r j) -> i j r", j=F)
                target = dots[:, :, first + a:first + BANK_SAMPLES:QUADS]
                last = copy(target, source)
            last.then_inc(done, 1)

        @block.scalar
        def _(act):
            def copy(target, source):
                return act.activation(target, source, ACT.Copy)

            def tile(turn, u):
                for g in range(NG):
                    if is_even(u, g):
                        copy_group(act, copy, turn, u, g, emb_act)
                copy_dots(act, copy, turn, u, 0, dots_act)

            def mlp(half):
                for n in range(N1):
                    act.wait_ge(h1_full, half * N1 + n // 2 * 2 + 2)
                    act.activation(h1[:, n, :], h1_ps[:, n, :], ACT.Relu,
                                   bias=b1_sb[:, n:n + 1]).then_inc(h1_ready, 1)
                for n in range(N2):
                    act.wait_ge(h2_full, half * N2 + n // 2 * 2 + 2)
                    act.activation(h2[:, n, :], h2_ps[:, n, :], ACT.Relu,
                                   bias=b2_sb[:, n:n + 1]).then_inc(h2_ready, 1)
                act.wait_ge(y_full, half + 1)
                act.activation(y_sb[:, bass.ds(half * HALF, HALF)], y_ps[0:1, 0:HALF], ACT.Copy).then_inc(y_ready, 1)

            for u in range(TILES_PER_TURN):
                tile(0, u)
            act.wait_ge(weights_in, WEIGHTS)
            with act.Fori(1, TURNS) as turn:
                tile(turn, 0)
                mlp(turn - 1)
                tile(turn, 1)
            mlp(TURNS - 1)

        @block.vector
        def _(dve):
            def copy(target, source):
                return dve.tensor_copy(target, source)

            def tile(turn, u):
                if count(turn):
                    dve.wait_ge(dots_full[1], tiles_before(turn - 1, u) + 1)
                copy(emb[:, u, :, F], x_sb[:, bass.ds(tiles_before(turn, u) * P, P)]).then_inc(emb_x, 1)
                for g in range(NG):
                    if not is_even(u, g):
                        copy_group(dve, copy, turn, u, g, emb_dve)
                copy_dots(dve, copy, turn, u, 1, dots_dve)

            dve.wait_ge(x_in, DMA)
            for u in range(TILES_PER_TURN):
                tile(0, u)
            with dve.Fori(1, TURNS) as turn:
                for u in range(TILES_PER_TURN):
                    tile(turn, u)


def kernel(**inputs):
    import numpy as np
    import concourse.bacc as bacc
    from concourse.bass_utils import run_bass_kernel_spmd

    n_tables = np.asarray(inputs["ids"]).shape[1]
    names = [f"tbl_{f}" for f in range(n_tables)]
    arrays = {name: np.ascontiguousarray(inputs[name]) for name in names + ["ids", "W_top1", "W_top2"]}
    arrays["x_t"] = np.ascontiguousarray(np.asarray(inputs["r_dense_x"]).T)
    arrays["b1"] = np.ascontiguousarray(np.asarray(inputs["b_top1"]).reshape(-1, P).T)
    arrays["b2"] = np.ascontiguousarray(np.asarray(inputs["b_top2"]).reshape(-1, P).T)
    arrays["w3"] = np.ascontiguousarray(np.asarray(inputs["W_top3"]).reshape(-1, P).T)
    arrays = {f"in_{name}": a for name, a in arrays.items()}

    nc = bacc.Bacc("TRN2", target_bir_lowering=False, num_devices=1)
    d = {name: nc.dram_tensor(name, a.shape, mybir.dt.from_np(a.dtype), kind="ExternalInput").ap()
         for name, a in arrays.items()}
    n_samples = arrays["in_ids"].shape[0]
    y = nc.dram_tensor("y", (1, n_samples), F32, kind="ExternalOutput").ap()
    dlrm_tower(nc, d["in_x_t"], d["in_ids"], [d[f"in_{name}"] for name in names], d["in_W_top1"], d["in_b1"],
               d["in_W_top2"], d["in_b2"], d["in_w3"], y)
    r = run_bass_kernel_spmd(nc, [arrays], core_ids=[0])
    return np.asarray(r.results[0]["y"]).reshape(n_samples, 1)
```

```python
from contextlib import ExitStack

import concourse.bass as bass
from concourse import mybir

F32 = mybir.dt.float32
F32R = mybir.dt.float32r
I32 = mybir.dt.int32
ALU = mybir.AluOpType
ACT = mybir.ActivationFunctionType

P = 128
DMA = 16
LOOKED_UP = 6
TILES_PER_TURN = 4
ROW_SLOTS = 2
GROUP = 4
QUADS = 4
ONEHOT_SLOTS = 4


def features_by_way(table_rows):
    by_size = sorted(range(len(table_rows)), key=lambda f: (table_rows[f], f))
    looked_up = sorted(by_size[:LOOKED_UP])
    return [f for f in range(len(table_rows)) if f not in looked_up], looked_up


def pair_blocks(features, chunk_rows):
    shapes = []

    def cover(first, n):
        if n <= 4:
            shapes.append((first, n - 1, first + 1, n - 1))
            return
        a = n // 2
        for j in range(0, n - a, chunk_rows // a):
            shapes.append((first, a, first + a + j, min(chunk_rows // a, n - a - j)))
        cover(first, a)
        cover(first + a, n - a)

    cover(0, features)
    shapes.sort(key=lambda b: -b[1] * b[3])
    used, blocks = [], []
    for i, n, j, m in shapes:
        fits = [c for c in range(len(used)) if used[c] + n * m <= chunk_rows]
        if not fits:
            fits = [len(used)]
            used.append(0)
        blocks.append((i, n, j, m, fits[0], used[fits[0]]))
        used[fits[0]] += n * m
    return blocks, used


def dlrm_tower(nc, x_t, ids, ids_looked, gathered, looked, w1, b1, w2, b2, w3, y_out):
    B = ids.shape[0]
    D = x_t.shape[0]
    NGATHER, NLOOK = len(gathered), len(looked)
    F = NGATHER + NLOOK
    NF = F + 1
    H1, H2 = w1.shape[1], w2.shape[1]
    N1, N2 = H1 // P, H2 // P
    TILES = B // P
    TURNS = TILES // TILES_PER_TURN
    TURN = TILES_PER_TURN * P
    HALF = 2 * P
    GROUPS = [list(range(f, min(f + GROUP, NGATHER))) for f in range(0, NGATHER, GROUP)]
    NG = len(GROUPS)
    BANK_SAMPLES = P // 2
    ROUNDS = BANK_SAMPLES // QUADS
    TABLE_P = 125
    CHUNKS = looked[0][1].shape[0] // TABLE_P
    ONEHOTS = NLOOK * CHUNKS
    assert D == P and TILES_PER_TURN == 4 and TILES % TILES_PER_TURN == 0 and NG % 2 == 1
    assert ROUNDS * F * 4 <= 2048 and CHUNKS % ONEHOT_SLOTS == 0
    assert all(table.shape[0] == TABLE_P * CHUNKS for _, table in looked)

    z_moves, k_rows = pair_blocks(NF, P)
    KZ = len(k_rows)
    MOVED = DMA * len(z_moves)

    with ExitStack() as ctx:
        def sb(name, shape, dt=F32):
            return ctx.enter_context(nc.sbuf_tensor(name, shape, dt))

        def psum(name, shape):
            return ctx.enter_context(nc.psum_tensor(name, shape, F32))

        def sem(name):
            return ctx.enter_context(nc.semaphore(name))

        identity = sb("identity", [P, P])
        x_sb = sb("x_sb", [P, 2, HALF])
        idx_all = sb("idx_all", [P, TILES, F], I32)
        idx = sb("idx", [P, ROW_SLOTS, F], I32)
        rows = sb("rows", [P, ROW_SLOTS, NGATHER, D])
        emb = sb("emb", [P, TILES_PER_TURN, P, NF])
        dots = sb("dots", [P, F * HALF])
        h1 = sb("h1", [P, N1 * HALF])
        dots_ijs = [dots[first:first + F, :].rearrange("i (j s) -> i j s", s=HALF) for first in (0, 32)]
        h1_nb = h1[:, :].rearrange("p (n b) -> p n b", b=HALF)
        z = sb("z", [P, KZ, HALF])
        w1_sb = sb("w1_sb", [P, KZ + 1, H1])
        w2_sb = sb("w2_sb", [P, N1, H2])
        w3_sb = sb("w3_sb", [P, N2])
        b1_sb = sb("b1_sb", [P, N1])
        b2_sb = sb("b2_sb", [P, N2])
        h2 = sb("h2", [P, N2, HALF])
        y_sb = sb("y_sb", [1, HALF])
        table_hi = sb("table_hi", [TABLE_P, NLOOK, CHUNKS * D], F32R)
        table_lo = sb("table_lo", [TABLE_P, NLOOK, CHUNKS * D], F32R)
        ids_sb = sb("ids_sb", [P, NLOOK, TURN], I32)
        row_of = sb("row_of", [P, CHUNKS])
        onehot = sb("onehot", [TABLE_P, ONEHOT_SLOTS, TURN], F32R)
        fit = F * HALF // (CHUNKS * D)
        raw = [(dots, k) if k < fit else (h1, k - fit) for k in range(NLOOK)]
        raw = [where[0:TABLE_P, k * CHUNKS * D:(k + 1) * CHUNKS * D] for where, k in raw]

        turned = [psum(f"turned{i}", [P, 512]) for i in range(2)]
        dot_ps = [psum(f"dot_ps{i}", [P, 512]) for i in range(2)]
        looked_ps = psum("looked_ps", [P, TURN])
        h1_ps = psum("h1_ps", [P, N1, HALF])
        h2_ps = psum("h2_ps", [P, N2, HALF])
        y_ps = h1_ps[0:1, 0, :]

        weights_in = sem("weights_in")
        x_in = [sem("x_in_even"), sem("x_in_odd")]
        identity_zero = sem("identity_zero")
        identity_ready = sem("identity_ready")
        row_of_ready = sem("row_of_ready")
        idx_in = sem("idx_in")
        idx_ready = sem("idx_ready")
        rows_in = [[sem(f"rows_in{v}_{g}") for g in range(NG)] for v in range(ROW_SLOTS)]
        table_in = [sem(f"table_in{k}") for k in range(NLOOK)]
        hi_ready = sem("hi_ready")
        lo_ready = sem("lo_ready")
        ids_in = sem("ids_in")
        onehot_ready = sem("onehot_ready")
        onehot_used = sem("onehot_used")
        looked_taken = sem("looked_taken")
        pool_steps = sem("pool_steps")
        sp_steps = sem("sp_steps")
        turned_full = sem("turned_full")
        emb_act = sem("emb_act")
        emb_dve = sem("emb_dve")
        emb_x = sem("emb_x")
        dots_full = [sem(f"dots_full{k}") for k in range(2)]
        dots_act = sem("dots_act")
        dots_dve = sem("dots_dve")
        z_in = sem("z_in")
        h1_full = sem("h1_full")
        h1_ready = sem("h1_ready")
        h2_full = sem("h2_full")
        h2_ready = sem("h2_ready")
        y_full = sem("y_full")
        y_ready = sem("y_ready")
        y_stored = [sem("y_stored_even"), sem("y_stored_odd")]

        def count(value):
            return not isinstance(value, int) or value > 0

        def tiles_before(turn, u):
            return turn * TILES_PER_TURN + u

        def halves_before(turn, u):
            return turn * (TILES_PER_TURN // 2) + u // 2

        def groups_before(turn, u, g):
            return turn * (TILES_PER_TURN * NG) + (u * NG + g)

        def even_groups_before(turn, u, g):
            return turn * (TILES_PER_TURN * NG // 2) + (u * NG + g + 1) // 2

        def odd_groups_before(turn, u, g):
            return turn * (TILES_PER_TURN * NG // 2) + (u * NG + g) // 2

        def is_even(u, g):
            return (u * NG + g) % 2 == 0

        block = ctx.enter_context(nc.Block())

        @block.sync
        def _(sp):
            def load_ids(turn):
                if count(turn):
                    sp.wait_ge(onehot_ready, turn * ONEHOTS)
                    sp.sem_inc(sp_steps, 1)
                sp.dma_start(ids_sb[:, :, :], ids_looked[:, bass.ds(turn * TURN, TURN)].partition_broadcast(P)) \
                    .then_inc(ids_in, DMA)

            def load_x(half, parity, wait=True):
                if wait:
                    sp.wait_ge(h1_full, (half - 1) * N1)
                    sp.sem_inc(sp_steps, 1)
                sp.dma_start(x_sb[:, parity, :], x_t[:, bass.ds(half * HALF, HALF)]).then_inc(x_in[parity], DMA)

            def move_pairs(half, parity):
                sp.wait_ge(dots_act, half * 2 + 2)
                sp.wait_ge(dots_dve, half * 2 + 2)
                sp.sem_inc(sp_steps, 1)
                if count(half):
                    sp.wait_ge(h1_full, half * N1)
                for i, n, j, m, chunk, row in z_moves:
                    sp.dma_start(z[row:row + n * m, chunk, :], dots_ijs[parity][i:i + n, j - 1:j - 1 + m, :]) \
                        .then_inc(z_in, DMA)

            def store_y(half, parity):
                sp.wait_ge(y_ready, half + 1)
                sp.sem_inc(sp_steps, 1)
                sp.dma_start(y_out[:, bass.ds(half * HALF, HALF)], y_sb[:, :]).then_inc(y_stored[parity], DMA)

            sp.dma_start(idx_all[:, :, :], ids.rearrange("(t p) f -> p t f", p=P)).then_inc(idx_in, DMA)
            load_ids(0)
            load_x(0, 0, wait=False)
            load_x(1, 1, wait=False)
            for c, k in enumerate(k_rows):
                sp.dma_start(w1_sb[0:k, c, :], w1[c * P:c * P + k, :]).then_inc(weights_in, DMA)
            sp.dma_start(w1_sb[:, KZ, :], w1[KZ * P:KZ * P + D, :]).then_inc(weights_in, DMA)
            sp.dma_start(w2_sb[:, :, :], w2.rearrange("(c p) n -> p c n", p=P)).then_inc(weights_in, DMA)
            sp.dma_start(w3_sb[:, :], w3).then_inc(weights_in, DMA)
            sp.dma_start(b1_sb[:, :], b1).then_inc(weights_in, DMA)
            sp.dma_start(b2_sb[:, :], b2).then_inc(weights_in, DMA)
            move_pairs(0, 0)
            with sp.Fori(1, TURNS) as turn:
                load_ids(turn)
                load_x(turn * 2, 0)
                move_pairs(turn * 2 - 1, 1)
                store_y(turn * 2 - 2, 0)
                load_x(turn * 2 + 1, 1)
                move_pairs(turn * 2, 0)
                store_y(turn * 2 - 1, 1)
            move_pairs(TURNS * 2 - 1, 1)
            store_y(TURNS * 2 - 2, 0)
            store_y(TURNS * 2 - 1, 1)
            sp.wait_ge(y_stored[0], DMA * TURNS)
            sp.wait_ge(y_stored[1], DMA * TURNS)

        WEIGHTS = DMA * (KZ + 1 + 4)

        @block.gpsimd
        def _(pool):
            pool.memset(identity[:, :], 0.0).then_inc(identity_zero, 1)
            pool.wait_ge(identity_zero, 1)
            pool.affine_select(out=identity[:, :], in_=identity[:, :], compare_op=ALU.not_equal, fill=1.0,
                               base=0, pattern=[[-1, P]], channel_multiplier=1).then_inc(identity_ready, 1)
            pool.iota(row_of[:, :], pattern=[[1, CHUNKS]], base=0, channel_multiplier=CHUNKS,
                      allow_small_or_imprecise_dtypes=True).then_inc(row_of_ready, 1)

            def gather(turn, u):
                v = u % ROW_SLOTS
                if count(groups_before(turn, u - ROW_SLOTS, NG)):
                    pool.wait_ge(turned_full, groups_before(turn, u - ROW_SLOTS, NG))
                    pool.sem_inc(pool_steps, 1)
                pool.tensor_copy(idx[:, v, :], idx_all[:, tiles_before(turn, u), :]).then_inc(idx_ready, 1)
                pool.wait_ge(idx_ready, tiles_before(turn, u) + 1)
                pool.sem_inc(pool_steps, 1)
                for g, group in enumerate(GROUPS):
                    for n in group:
                        feature, table = gathered[n]
                        pool.indirect_dma_start(
                            out=rows[:, v, n, :], out_offset=None, in_=table,
                            in_offset=bass.IndirectOffsetOnAxis(ap=idx[:, v, feature:feature + 1], axis=0),
                        ).then_inc(rows_in[v][g], DMA)

            pool.wait_ge(idx_in, DMA)
            for u in range(TILES_PER_TURN):
                gather(0, u)
            with pool.Fori(1, TURNS) as turn:
                for u in range(TILES_PER_TURN):
                    gather(turn, u)

        @block.tensor
        def _(pe):
            def look_up(turn):
                for k in range(NLOOK):
                    if count(turn * NLOOK + k):
                        pe.wait_ge(looked_taken, turn * NLOOK + k)
                    if isinstance(turn, int):
                        pe.wait_ge(hi_ready, k + 1)
                        pe.wait_ge(lo_ready, k + 1)
                    for c in range(CHUNKS):
                        slot = onehot[:, c % ONEHOT_SLOTS, :]
                        pe.wait_ge(onehot_ready, turn * ONEHOTS + (k * CHUNKS + c + 1))
                        pe.matmul(looked_ps[:, :], table_hi[:, k, c * D:(c + 1) * D], slot,
                                  start=c == 0, stop=False)
                        last = pe.matmul(looked_ps[:, :], table_lo[:, k, c * D:(c + 1) * D], slot,
                                         start=False, stop=c == CHUNKS - 1)
                        last.then_inc(onehot_used, 1)

            def transpose_tile(turn, u):
                v = u % ROW_SLOTS
                for g, group in enumerate(GROUPS):
                    pe.wait_ge(rows_in[v][g], halves_before(turn, u) * (DMA * len(group)) + DMA * len(group))
                    if is_even(u, g):
                        bank, taken, before = turned[0], emb_act, even_groups_before(turn, u, g)
                    else:
                        bank, taken, before = turned[1], emb_dve, odd_groups_before(turn, u, g)
                    if count(before):
                        pe.wait_ge(taken, before)
                    for n, f in enumerate(group):
                        last = pe.transpose(bank[:, n * P:(n + 1) * P], rows[:, v, f, :], identity[:, :])
                    last.then_inc(turned_full, 1)

            def dot_tile(turn, u):
                if u == 0:
                    pe.wait_ge(looked_taken, turn * NLOOK + NLOOK)
                pe.wait_ge(emb_act, even_groups_before(turn, u, NG))
                pe.wait_ge(emb_dve, odd_groups_before(turn, u, NG))
                pe.wait_ge(emb_x, tiles_before(turn, u) + 1)
                for k, taken in enumerate((dots_act, dots_dve)):
                    before = tiles_before(turn, u)
                    if count(before):
                        pe.wait_ge(taken, before)
                    for r in range(ROUNDS):
                        for a in range(QUADS):
                            s = k * BANK_SAMPLES + r * QUADS + a
                            last = pe.matmul(dot_ps[k][32 * a:32 * a + F, r * F:(r + 1) * F],
                                             emb[:, u, s, 0:F], emb[:, u, s, 1:NF], start=True, stop=True)
                    last.then_inc(dots_full[k], 1)

            def mlp(half, parity):
                pe.wait_ge(z_in, half * MOVED + MOVED)
                for n in range(N1):
                    for c, k in enumerate(k_rows):
                        pe.matmul(h1_ps[:, n, :], w1_sb[0:k, c, n * P:(n + 1) * P], z[0:k, c, :],
                                  start=c == 0, stop=False)
                    pe.matmul(h1_ps[:, n, :], w1_sb[:, KZ, n * P:(n + 1) * P], x_sb[:, parity, :],
                              start=False, stop=True).then_inc(h1_full, 1)
                for n in range(N2):
                    for c in range(N1):
                        if n == 0:
                            pe.wait_ge(h1_ready, half * N1 + c + 1)
                        last = pe.matmul(h2_ps[:, n, :], w2_sb[:, c, n * P:(n + 1) * P], h1_nb[:, c, :],
                                         start=c == 0, stop=c == N1 - 1)
                    last.then_inc(h2_full, 1)
                for c in range(N2):
                    pe.wait_ge(h2_ready, half * N2 + c + 1)
                    last = pe.matmul(y_ps, w3_sb[:, c:c + 1], h2[:, c, :], start=c == 0, stop=c == N2 - 1)
                last.then_inc(y_full, 1)

            pe.wait_ge(identity_ready, 1)
            look_up(0)
            for u in range(TILES_PER_TURN):
                transpose_tile(0, u)
                dot_tile(0, u)
            pe.wait_ge(weights_in, WEIGHTS)
            mlp(0, 0)
            with pe.Fori(1, TURNS) as turn:
                look_up(turn)
                for u in range(TILES_PER_TURN):
                    transpose_tile(turn, u)
                    dot_tile(turn, u)
                    if u == 1:
                        mlp(turn * 2 - 1, 1)
                mlp(turn * 2, 0)
            pe.wait_ge(y_ready, TURNS * 2 - 1)
            mlp(TURNS * 2 - 1, 1)

        def copy_group(eng, copy, turn, u, g, done):
            eng.wait_ge(turned_full, groups_before(turn, u, g) + 1)
            if g < 2:
                if count(turn):
                    eng.wait_ge(dots_full[1], tiles_before(turn - 1, u) + 1)
            group = GROUPS[g]
            source = turned[0 if is_even(u, g) else 1][:, 0:len(group) * P].rearrange("d (f s) -> d f s", s=P)
            target = emb[:, u, :, group[0]:group[-1] + 1].rearrange("d s f -> d f s")
            copy(target, source).then_inc(done, 1)

        def copy_dots(eng, copy, turn, u, k, done):
            eng.wait_ge(dots_full[k], tiles_before(turn, u) + 1)
            half = halves_before(turn, u)
            if u % 2 == 0 and count(half - 1):
                eng.wait_ge(z_in, (half - 1) * MOVED)
            first = (u % 2) * P + k * BANK_SAMPLES
            for a in range(QUADS):
                source = dot_ps[k][32 * a:32 * a + F, 0:ROUNDS * F].rearrange("i (r j) -> i j r", j=F)
                target = dots_ijs[u // 2][:, :, first + a:first + BANK_SAMPLES:QUADS]
                last = copy(target, source)
            last.then_inc(done, 1)

        @block.scalar
        def _(act):
            def copy(target, source):
                return act.activation(target, source, ACT.Copy)

            def take_looked_up(turn):
                for k in range(NLOOK):
                    act.wait_ge(onehot_used, turn * ONEHOTS + (k + 1) * CHUNKS)
                    if k == 0 and count(turn):
                        act.wait_ge(dots_full[1], tiles_before(turn, 0))
                    source = looked_ps[:, :].rearrange("d (u s) -> d u s", s=P)
                    copy(emb[:, :, :, NGATHER + k], source).then_inc(looked_taken, 1)

            def tile(turn, u):
                for g in range(NG):
                    if is_even(u, g):
                        copy_group(act, copy, turn, u, g, emb_act)
                copy_dots(act, copy, turn, u, 0, dots_act)

            def mlp(turn, parity):
                half = turn * 2 + parity
                for n in range(N1):
                    act.wait_ge(h1_full, half * N1 + (n // 2 * 2 + 2))
                    act.activation(h1_nb[:, n, :], h1_ps[:, n, :], ACT.Relu,
                                   bias=b1_sb[:, n:n + 1]).then_inc(h1_ready, 1)
                for n in range(N2):
                    act.wait_ge(h2_full, half * N2 + (n // 2 * 2 + 2))
                    act.activation(h2[:, n, :], h2_ps[:, n, :], ACT.Relu,
                                   bias=b2_sb[:, n:n + 1]).then_inc(h2_ready, 1)
                act.wait_ge(y_full, half + 1)
                if count(turn + parity):
                    act.wait_ge(y_stored[1 - parity], (turn + parity) * DMA)
                act.activation(y_sb[:, :], y_ps, ACT.Copy).then_inc(y_ready, 1)

            for k, (_, table) in enumerate(looked):
                act.dma_start(raw[k], table.rearrange("(p c) d -> p (c d)", c=CHUNKS)).then_inc(table_in[k], DMA)
            for k in range(NLOOK):
                act.wait_ge(table_in[k], DMA)
                copy(table_hi[:, k, :], raw[k]).then_inc(hi_ready, 1)
            take_looked_up(0)
            for u in range(TILES_PER_TURN):
                tile(0, u)
            act.wait_ge(weights_in, WEIGHTS)
            mlp(0, 0)
            with act.Fori(1, TURNS) as turn:
                take_looked_up(turn)
                for u in range(TILES_PER_TURN):
                    tile(turn, u)
                    if u == 1:
                        mlp(turn - 1, 1)
                mlp(turn, 0)
            mlp(TURNS - 1, 1)

        @block.vector
        def _(dve):
            def copy(target, source):
                return dve.tensor_copy(target, source)

            def make_onehots(turn):
                dve.wait_ge(ids_in, turn * DMA + DMA)
                for n in range(ONEHOTS):
                    k, c = divmod(n, CHUNKS)
                    if isinstance(turn, int) and c == 0:
                        dve.wait_ge(hi_ready, k + 1)
                        dve.tensor_tensor(table_lo[:, k, :], raw[k], table_hi[:, k, :].bitcast(F32),
                                          ALU.subtract).then_inc(lo_ready, 1)
                    if count(turn * ONEHOTS + (n + 1 - ONEHOT_SLOTS)):
                        dve.wait_ge(onehot_used, turn * ONEHOTS + (n + 1 - ONEHOT_SLOTS))
                    dve.tensor_scalar(onehot[:, c % ONEHOT_SLOTS, :], ids_sb[0:TABLE_P, k, :],
                                      row_of[0:TABLE_P, c:c + 1], None, ALU.is_equal).then_inc(onehot_ready, 1)

            def tile(turn, u):
                dve.wait_ge(x_in[u // 2], turn * DMA + DMA)
                if count(turn):
                    dve.wait_ge(dots_full[1], tiles_before(turn - 1, u) + 1)
                copy(emb[:, u, :, F], x_sb[:, u // 2, (u % 2) * P:(u % 2 + 1) * P]).then_inc(emb_x, 1)
                for g in range(NG):
                    if not is_even(u, g):
                        copy_group(dve, copy, turn, u, g, emb_dve)
                copy_dots(dve, copy, turn, u, 1, dots_dve)

            dve.wait_ge(row_of_ready, 1)
            make_onehots(0)
            for u in range(TILES_PER_TURN):
                tile(0, u)
            with dve.Fori(1, TURNS) as turn:
                make_onehots(turn)
                for u in range(TILES_PER_TURN):
                    tile(turn, u)


def kernel(**inputs):
    import numpy as np
    import concourse.bacc as bacc
    from concourse.bass_utils import run_bass_kernel_spmd

    ids = np.asarray(inputs["ids"])
    n_samples, n_tables = ids.shape
    names = [f"tbl_{f}" for f in range(n_tables)]
    arrays = {name: np.ascontiguousarray(inputs[name]) for name in names + ["ids", "W_top2"]}
    gathered, looked_up = features_by_way([arrays[name].shape[0] for name in names])
    order = gathered + looked_up + [n_tables]
    row = {pair: n for n, pair in enumerate(zip(*np.triu_indices(n_tables + 1, k=1)))}
    blocks, used = pair_blocks(n_tables + 1, P)
    w_top1 = np.asarray(inputs["W_top1"])
    w1 = np.zeros(((len(used) + 1) * P, w_top1.shape[1]), w_top1.dtype)
    for i, n, j, m, chunk, first in blocks:
        for a in range(n):
            for b in range(m):
                if i + a < j + b:
                    pair = order[i + a], order[j + b]
                    w1[chunk * P + first + a * m + b] = w_top1[row[min(pair), max(pair)]]
    w1[len(used) * P:] = w_top1[len(row):]
    arrays["w1"] = w1
    arrays["ids_looked"] = np.ascontiguousarray(ids.T[np.array(looked_up)])
    arrays["x_t"] = np.ascontiguousarray(np.asarray(inputs["r_dense_x"]).T)
    arrays["b1"] = np.ascontiguousarray(np.asarray(inputs["b_top1"]).reshape(-1, P).T)
    arrays["b2"] = np.ascontiguousarray(np.asarray(inputs["b_top2"]).reshape(-1, P).T)
    arrays["w3"] = np.ascontiguousarray(np.asarray(inputs["W_top3"]).reshape(-1, P).T)
    arrays = {f"in_{name}": a for name, a in arrays.items()}

    nc = bacc.Bacc("TRN2", target_bir_lowering=False, num_devices=1)
    d = {name: nc.dram_tensor(name, a.shape, mybir.dt.from_np(a.dtype), kind="ExternalInput").ap()
         for name, a in arrays.items()}
    y = nc.dram_tensor("y", (1, n_samples), F32, kind="ExternalOutput").ap()
    dlrm_tower(nc, d["in_x_t"], d["in_ids"], d["in_ids_looked"], [(f, d[f"in_tbl_{f}"]) for f in gathered],
               [(f, d[f"in_tbl_{f}"]) for f in looked_up], d["in_w1"], d["in_b1"], d["in_W_top2"], d["in_b2"],
               d["in_w3"], y)
    r = run_bass_kernel_spmd(nc, [arrays], core_ids=[0])
    return np.asarray(r.results[0]["y"]).reshape(n_samples, 1)
```

```python
from contextlib import ExitStack

import concourse.bass as bass
from concourse import mybir

F32 = mybir.dt.float32
F32R = mybir.dt.float32r
I32 = mybir.dt.int32
ALU = mybir.AluOpType
ACT = mybir.ActivationFunctionType

P = 128
DMA = 16
LOOKED_UP = 8
TILES_PER_TURN = 4
ROW_SLOTS = 2
GROUP = 4
QUADS = 4
ONEHOT_SLOTS = 4
ID_SLOTS = 3


def features_by_way(table_rows):
    by_size = sorted(range(len(table_rows)), key=lambda f: (table_rows[f], f))
    looked_up = by_size[:LOOKED_UP]
    return [f for f in range(len(table_rows)) if f not in looked_up], looked_up


def pair_blocks(features, chunk_rows):
    shapes = [(i, min(3, features - 1 - i), i + 1, features - 1 - i) for i in range(0, features - 1, 3)]
    shapes.sort(key=lambda b: -b[1] * b[3])
    used = [0] * -(-sum(n * m for _, n, _, m in shapes) // chunk_rows)
    blocks = []
    for i, n, j, m in shapes:
        while m > 0:
            fits = [c for c in range(len(used)) if used[c] + n * m <= chunk_rows]
            c = fits[0] if fits else used.index(min(used))
            part = min(m, (chunk_rows - used[c]) // n)
            blocks.append((i, n, j, part, c, used[c]))
            used[c] += n * part
            j, m = j + part, m - part
    assert all(b[3] > 0 for b in blocks)
    return blocks, used


def dlrm_tower(nc, x_t, ids, ids_looked, gathered, looked, w1, b1, w2, b2, w3, y_out):
    B = ids.shape[0]
    D = x_t.shape[0]
    NGATHER, NLOOK = len(gathered), len(looked)
    F = NGATHER + NLOOK
    NF = F + 1
    H1, H2 = w1.shape[1], w2.shape[1]
    N1, N2 = H1 // P, H2 // P
    TILES = B // P
    TURNS = TILES // TILES_PER_TURN
    TURN = TILES_PER_TURN * P
    HALF = 2 * P
    GROUPS = [list(range(f, min(f + GROUP, NGATHER))) for f in range(0, NGATHER, GROUP)]
    NG = len(GROUPS)
    BANK_SAMPLES = P // 2
    ROUNDS = BANK_SAMPLES // QUADS
    TABLE_P = 125
    chunks = [table.shape[0] // TABLE_P for _, table in looked]
    ONEHOTS = sum(chunks)
    before_feature = [sum(chunks[:k]) for k in range(NLOOK)]
    assert D == P and TILES_PER_TURN == 4 and TILES % TILES_PER_TURN == 0 and NG == 5
    assert ROUNDS * F * 4 <= 2048 and chunks[0] >= ONEHOT_SLOTS and chunks[1] == 8 and NLOOK > ID_SLOTS and TURNS >= 3
    assert all(table.shape[0] == TABLE_P * n for n, (_, table) in zip(chunks, looked))

    z_moves, k_rows = pair_blocks(NF, P)
    k_rows.append(D)
    KZ = len(k_rows)
    assert N1 == 4 and KZ == 4 and N1 * N2 == 8
    MOVED = DMA * (len(z_moves) + 1)

    with ExitStack() as ctx:
        def sb(name, shape, dt=F32):
            return ctx.enter_context(nc.sbuf_tensor(name, shape, dt))

        def psum(name, shape):
            return ctx.enter_context(nc.psum_tensor(name, shape, F32))

        def sem(name):
            return ctx.enter_context(nc.semaphore(name))

        identity = sb("identity", [P, P])
        x_sb = sb("x_sb", [P, 2, HALF])
        idx_all = sb("idx_all", [P, TILES, F], I32)
        idx = sb("idx", [P, TILES_PER_TURN, F], I32)
        rows = sb("rows", [P, ROW_SLOTS, NGATHER, D])
        emb = sb("emb", [P, TILES_PER_TURN, P, NF])
        dots = sb("dots", [P, F * HALF])
        h1 = sb("h1", [P, N1 * HALF])
        dots_ijs = [dots[first:first + F, :].rearrange("i (j s) -> i j s", s=HALF) for first in (0, 32)]
        h1_nb = h1[:, :].rearrange("p (n b) -> p n b", b=HALF)
        z = sb("z", [P, 2, KZ, HALF])
        w1_sb = sb("w1_sb", [P, KZ, H1])
        w2_sb = sb("w2_sb", [P, N1, H2])
        w3_sb = sb("w3_sb", [P, N2])
        b1_sb = sb("b1_sb", [P, N1])
        b2_sb = sb("b2_sb", [P, N2])
        h2 = h1[:, 0:N2 * HALF].rearrange("p (n b) -> p n b", b=HALF)
        y_sb = dots[64:65, 0:HALF]
        table_hi = sb("table_hi", [TABLE_P, ONEHOTS * D], F32R)
        table_lo = sb("table_lo", [TABLE_P, ONEHOTS * D], F32R)
        ids_sb = sb("ids_sb", [P, ID_SLOTS, TURN], I32)
        sizes = sorted(set(chunks))
        row_of = sb("row_of", [P, sum(sizes)])
        row_ofs = {n: row_of[:, sum(sizes[:i]):sum(sizes[:i + 1])] for i, n in enumerate(sizes)}
        onehot = sb("onehot", [TABLE_P, ONEHOT_SLOTS, TURN], F32R)
        raw, room = [], [dots[:, :], h1[:, :], z[:, :, :, :].rearrange("p t c b -> p (t c b)")]
        used = 0
        for k in range(NLOOK):
            if used + chunks[k] * D > room[0].shape[1]:
                room, used = room[1:], 0
            raw.append(room[0][0:TABLE_P, used:used + chunks[k] * D])
            used += chunks[k] * D
        columns_of = [slice(before_feature[k] * D, (before_feature[k] + chunks[k]) * D) for k in range(NLOOK)]

        turned = [psum(f"turned{i}", [P, 512]) for i in range(2)]
        dot_ps = [psum(f"dot_ps{i}", [P, 512]) for i in range(2)]
        looked_ps = psum("looked_ps", [P, TURN])
        h1_ps = psum("h1_ps", [P, N1, HALF])
        h2_ps = psum("h2_ps", [P, N2, HALF])
        h2_flat = h2_ps[:, :, :].rearrange("p n b -> p (n b)")
        y_ps = [looked_ps[0:1, 0:HALF], h1_ps[0:1, 0, :]]

        weights_in = sem("weights_in")
        x_in = [sem("x_in_even"), sem("x_in_odd")]
        identity_zero = sem("identity_zero")
        identity_ready = sem("identity_ready")
        row_of_ready = sem("row_of_ready")
        idx_in_first, idx_in = sem("idx_in_first"), sem("idx_in")
        idx_ready = sem("idx_ready")
        rows_in = [[sem(f"rows_in{v}_{g}") for g in range(NG)] for v in range(ROW_SLOTS)]
        table_in = [sem(f"table_in{k}") for k in range(NLOOK)]
        hi_ready = sem("hi_ready")
        lo_ready = sem("lo_ready")
        ids_in = [sem(f"ids_in{i}") for i in range(ID_SLOTS)]
        onehot_ready = sem("onehot_ready")
        onehot_used = sem("onehot_used")
        looked_taken = sem("looked_taken")
        pool_steps = sem("pool_steps")
        sp_steps = sem("sp_steps")
        turned_full = sem("turned_full")
        emb_act = sem("emb_act")
        emb_dve = sem("emb_dve")
        emb_x = sem("emb_x")
        dots_full = [sem(f"dots_full{k}") for k in range(2)]
        dots_act = sem("dots_act")
        dots_dve = sem("dots_dve")
        z_in = [sem("z_in_even"), sem("z_in_odd")]
        h1_full = sem("h1_full")
        h1_ready = sem("h1_ready")
        h2_full = sem("h2_full")
        h2_ready = sem("h2_ready")
        y_full = sem("y_full")
        y_ready = sem("y_ready")
        y_stored = [sem("y_stored_even"), sem("y_stored_odd")]

        def count(value):
            return not isinstance(value, int) or value > 0

        def tiles_before(turn, u):
            return turn * TILES_PER_TURN + u

        def halves_before(turn, u):
            return turn * (TILES_PER_TURN // 2) + u // 2

        def groups_before(turn, u, g):
            return turn * (TILES_PER_TURN * NG) + (u * NG + g)

        def even_groups_before(turn, u, g):
            return turn * (TILES_PER_TURN * NG // 2) + (u * NG + g + 1) // 2

        def odd_groups_before(turn, u, g):
            return turn * (TILES_PER_TURN * NG // 2) + (u * NG + g) // 2

        def is_even(u, g):
            return (u * NG + g) % 2 == 0

        looked_banks = [looked_ps[:, :], h2_flat]
        last_in_bank = [max(k for k in range(NLOOK) if k % 2 == bank) - NLOOK for bank in range(2)]

        def looked_before(turn, k):
            return turn * NLOOK + ((k - 2 if k >= 2 else last_in_bank[k]) + 1)


        block = ctx.enter_context(nc.Block())

        @block.sync
        def _(sp):
            def load_x(turn, parity):
                half = turn * 2 + parity
                if count(turn):
                    sp.wait_ge(emb_x, turn * TILES_PER_TURN + (2 * parity + 2 - TILES_PER_TURN))
                    sp.sem_inc(sp_steps, 1)
                sp.dma_start(x_sb[:, parity, :], x_t[:, bass.ds(half * HALF, HALF)]).then_inc(x_in[parity], DMA)

            def move_pairs(turn, parity):
                half = turn * 2 + parity
                if count(half - 1):
                    sp.wait_ge(h1_full, (half - 1) * N1)
                    sp.sem_inc(sp_steps, 1)
                else:
                    sp.wait_ge(lo_ready, NLOOK)
                sp.dma_start(z[:, parity, KZ - 1, :], x_t[:, bass.ds(half * HALF, HALF)]).then_inc(z_in[parity], DMA)
                sp.wait_ge(dots_act, half * 2 + 2)
                sp.wait_ge(dots_dve, half * 2 + 2)
                sp.sem_inc(sp_steps, 1)
                for i, n, j, m, chunk, row in z_moves:
                    sp.dma_start(z[row:row + n * m, parity, chunk, :], dots_ijs[parity][i:i + n, j - 1:j - 1 + m, :]) \
                        .then_inc(z_in[parity], DMA)

            def store_y(turn, parity):
                half = turn * 2 + parity
                sp.wait_ge(y_ready, half + 1)
                sp.sem_inc(sp_steps, 1)
                sp.dma_start(y_out[:, bass.ds(half * HALF, HALF)], y_sb).then_inc(y_stored[parity], DMA)

            ids_tpf = ids.rearrange("(t p) f -> p t f", p=P)
            sp.dma_start(idx_all[:, 0:1, :], ids_tpf[:, 0:1, :]).then_inc(idx_in_first, DMA)
            sp.dma_start(idx_all[:, 1:TILES, :], ids_tpf[:, 1:TILES, :]).then_inc(idx_in, DMA)
            load_x(0, 0)
            sp.wait_ge(hi_ready, NLOOK)
            load_x(0, 1)
            for c, k in enumerate(k_rows):
                sp.dma_start(w1_sb[0:k, c, :], w1[c * P:c * P + k, :]).then_inc(weights_in, DMA)
            sp.dma_start(w2_sb[:, :, :], w2.rearrange("(c p) n -> p c n", p=P)).then_inc(weights_in, DMA)
            sp.dma_start(w3_sb[:, :], w3).then_inc(weights_in, DMA)
            sp.dma_start(b1_sb[:, :], b1).then_inc(weights_in, DMA)
            sp.dma_start(b2_sb[:, :], b2).then_inc(weights_in, DMA)
            move_pairs(0, 0)

            def turn_of(turn):
                load_x(turn, 0)
                load_x(turn, 1)
                move_pairs(turn - 1, 1)
                if count(turn - 1):
                    store_y(turn - 2, 1)
                move_pairs(turn, 0)
                store_y(turn - 1, 0)

            turn_of(1)
            with sp.Fori(2, TURNS) as turn:
                turn_of(turn)
            move_pairs(TURNS - 1, 1)
            store_y(TURNS - 2, 1)
            store_y(TURNS - 1, 0)
            store_y(TURNS - 1, 1)
            sp.wait_ge(y_stored[0], DMA * TURNS)
            sp.wait_ge(y_stored[1], DMA * TURNS)

        WEIGHTS = DMA * (KZ + 4)

        @block.gpsimd
        def _(pool):
            pool.memset(identity[:, :], 0.0).then_inc(identity_zero, 1)
            pool.wait_ge(identity_zero, 1)
            pool.affine_select(out=identity[:, :], in_=identity[:, :], compare_op=ALU.not_equal, fill=1.0,
                               base=0, pattern=[[-1, P]], channel_multiplier=1).then_inc(identity_ready, 1)
            for n in sizes:
                pool.iota(row_ofs[n], pattern=[[1, n]], base=0, channel_multiplier=n,
                          allow_small_or_imprecise_dtypes=True).then_inc(row_of_ready, 1)

            def gather(turn, u):
                v = u % ROW_SLOTS
                if count(turn):
                    index = idx[:, u, :]
                    pool.wait_ge(idx_ready, tiles_before(turn - 1, u) + 1)
                    pool.sem_inc(pool_steps, 1)
                else:
                    index = idx_all[:, u, :]
                for g, group in enumerate(GROUPS):
                    before = groups_before(turn, u - ROW_SLOTS, g) + 1
                    if count(before):
                        pool.wait_ge(turned_full, before)
                        pool.sem_inc(pool_steps, 1)
                    for n in group:
                        feature, table = gathered[n]
                        pool.indirect_dma_start(
                            out=rows[:, v, n, :], out_offset=None, in_=table,
                            in_offset=bass.IndirectOffsetOnAxis(ap=index[:, feature:feature + 1], axis=0),
                        ).then_inc(rows_in[v][g], DMA)

            pool.wait_ge(idx_in_first, DMA)
            gather(0, 0)
            pool.wait_ge(idx_in, DMA)
            for u in range(1, TILES_PER_TURN):
                gather(0, u)
            with pool.Fori(1, TURNS) as turn:
                for u in range(TILES_PER_TURN):
                    gather(turn, u)

        @block.tensor
        def _(pe):
            def look_up(turn, k, part=None):
                bank = looked_banks[k % 2]
                part = range(chunks[k]) if part is None else part
                if part[0] == 0:
                    before = looked_before(turn, k)
                    if count(before):
                        pe.wait_ge(looked_taken, before)
                    if not count(turn):
                        pe.wait_ge(hi_ready, k + 1)
                        pe.wait_ge(lo_ready, k + 1)
                for c in part:
                    n = before_feature[k] + c
                    slot = onehot[:, c % ONEHOT_SLOTS, :]
                    pe.wait_ge(onehot_ready, turn * ONEHOTS + (n + 1))
                    pe.matmul(bank, table_hi[:, n * D:(n + 1) * D], slot, start=c == 0, stop=False)
                    pe.matmul(bank, table_lo[:, n * D:(n + 1) * D], slot,
                              start=False, stop=c == chunks[k] - 1).then_inc(onehot_used, 1)

            def transpose_group(turn, u, g):
                group, v = GROUPS[g], u % ROW_SLOTS
                pe.wait_ge(rows_in[v][g], halves_before(turn, u) * (DMA * len(group)) + DMA * len(group))
                if is_even(u, g):
                    bank, taken, before = turned[0], emb_act, even_groups_before(turn, u, g)
                else:
                    bank, taken, before = turned[1], emb_dve, odd_groups_before(turn, u, g)
                if count(before):
                    pe.wait_ge(taken, before)
                for n, f in enumerate(group):
                    last = pe.transpose(bank[:, n * P:(n + 1) * P], rows[:, v, f, :], identity[:, :])
                last.then_inc(turned_full, 1)

            def dot_quarter(turn, u, q, step=None):
                k = q // 2
                for n in range(ROUNDS // 2 * QUADS):
                    if step is not None and n == 0:
                        for i in range(4):
                            step(4 * q + i)
                    if n == 0 and q == 0:
                        pe.wait_ge(looked_taken, turn * NLOOK + NLOOK)
                        pe.wait_ge(emb_act, even_groups_before(turn, u, NG))
                        pe.wait_ge(emb_dve, odd_groups_before(turn, u, NG))
                        pe.wait_ge(emb_x, tiles_before(turn, u) + 1)
                    if n == 0 and q % 2 == 0 and count(tiles_before(turn, u)):
                        pe.wait_ge((dots_act, dots_dve)[k], tiles_before(turn, u))
                    r, a = ROUNDS // 2 * (q % 2) + n // QUADS, n % QUADS
                    s = k * BANK_SAMPLES + r * QUADS + a
                    last = pe.matmul(dot_ps[k][32 * a:32 * a + F, r * F:(r + 1) * F],
                                     emb[:, u, s, 0:F], emb[:, u, s, 1:NF], start=True, stop=True)
                if q % 2 == 1:
                    last.then_inc(dots_full[k], 1)

            def dot_tile(turn, u, step):
                for q in range(4):
                    dot_quarter(turn, u, q, step)

            def transpose_and_dot(turn, u, dots_u, step):
                for g in range(NG):
                    transpose_group(turn, u, g)
                    if g < 4:
                        dot_quarter(turn, dots_u, g, step)

            def transpose_and_look_up(turn, u, k):
                for g in range(NG):
                    transpose_group(turn, u, g)
                    if g < 4:
                        look_up(turn, k, range(2 * g, 2 * g + 2))

            def layer1_step(turn, parity, n):
                block, c = n // KZ, n % KZ
                k = k_rows[c]
                if n == 0:
                    pe.wait_ge(z_in[parity], turn * MOVED + MOVED)
                last = pe.matmul(h1_ps[:, block, :], w1_sb[0:k, c, block * P:(block + 1) * P], z[0:k, parity, c, :],
                                 start=c == 0, stop=c == KZ - 1)
                if c == KZ - 1:
                    last.then_inc(h1_full, 1)

            def layer2_step(turn, parity, n):
                if n < N1 * N2:
                    block, c = n // N1, n % N1
                    if block == 0:
                        pe.wait_ge(h1_ready, turn * (2 * N1) + (parity * N1 + c + 1))
                    last = pe.matmul(h2_ps[:, block, :], w2_sb[:, c, block * P:(block + 1) * P], h1_nb[:, c, :],
                                     start=c == 0, stop=c == N1 - 1)
                    if c == N1 - 1:
                        last.then_inc(h2_full, 1)

            def layer3(turn, parity):
                for c in range(N2):
                    pe.wait_ge(h2_ready, turn * (2 * N2) + (parity * N2 + c + 1))
                    last = pe.matmul(y_ps[parity], w3_sb[:, c:c + 1], h2[:, c, :], start=c == 0, stop=c == N2 - 1)
                last.then_inc(y_full, 1)

            def handle(turn, last=False):
                if count(turn):
                    steps = [lambda n: layer1_step(turn - 1, 0, n), lambda n: layer2_step(turn - 1, 0, n),
                             lambda n: layer1_step(turn - 1, 1, n), lambda n: layer2_step(turn - 1, 1, n)]
                else:
                    steps = [None] * 4
                transpose_and_look_up(turn, 0, 1)
                for k in range(2, NLOOK):
                    look_up(turn, k)
                transpose_and_dot(turn, 1, 0, steps[0])
                transpose_and_dot(turn, 2, 1, steps[1])
                if count(turn):
                    layer3(turn - 1, 0)
                for g in range(4):
                    transpose_group(turn, 3, g)
                    dot_quarter(turn, 2, g, steps[2])
                if not last:
                    if count(turn):
                        pe.wait_ge(y_ready, turn * 2 - 1)
                    look_up(turn + 1, 0)
                transpose_group(turn, 3, 4)
                dot_tile(turn, 3, steps[3])
                if count(turn):
                    layer3(turn - 1, 1)
                else:
                    pe.wait_ge(weights_in, WEIGHTS)

            look_up(0, 0)
            pe.wait_ge(identity_ready, 1)
            handle(0)
            with pe.Fori(1, TURNS - 1) as turn:
                handle(turn)
            handle(TURNS - 1, last=True)
            pe.wait_ge(y_ready, TURNS * 2 - 2)
            for parity in range(2):
                for n in range(N1 * KZ):
                    layer1_step(TURNS - 1, parity, n)
                for n in range(N1 * N2):
                    layer2_step(TURNS - 1, parity, n)
                layer3(TURNS - 1, parity)

        def copy_group(eng, copy, turn, u, g, done):
            eng.wait_ge(turned_full, groups_before(turn, u, g) + 1)
            if g < 2:
                if count(turn):
                    eng.wait_ge(dots_full[1], tiles_before(turn - 1, u) + 1)
            group = GROUPS[g]
            source = turned[0 if is_even(u, g) else 1][:, 0:len(group) * P].rearrange("d (f s) -> d f s", s=P)
            target = emb[:, u, :, group[0]:group[-1] + 1].rearrange("d s f -> d f s")
            copy(target, source).then_inc(done, 1)

        def copy_dots(eng, copy, turn, u, k, done):
            eng.wait_ge(dots_full[k], tiles_before(turn, u) + 1)
            if u % 2 == 0 and count(turn):
                eng.wait_ge(z_in[u // 2], turn * MOVED)
            first = (u % 2) * P + k * BANK_SAMPLES
            for a in range(QUADS):
                source = dot_ps[k][32 * a:32 * a + F, 0:ROUNDS * F].rearrange("i (r j) -> i j r", j=F)
                target = dots_ijs[u // 2][:, :, first + a:first + BANK_SAMPLES:QUADS]
                last = copy(target, source)
            last.then_inc(done, 1)

        @block.scalar
        def _(act):
            def copy(target, source):
                return act.activation(target, source, ACT.Copy)

            def load_ids(turn, k):
                act.dma_start(ids_sb[:, k % ID_SLOTS, :],
                              ids_looked[k:k + 1, bass.ds(turn * TURN, TURN)].partition_broadcast(P)) \
                    .then_inc(ids_in[k % ID_SLOTS], DMA)

            def take_looked_up(turn, k, last):
                act.wait_ge(onehot_used, turn * ONEHOTS + (before_feature[k] + chunks[k]))
                if k == 0 and count(turn):
                    act.wait_ge(dots_full[1], tiles_before(turn, 0))
                source = looked_banks[k % 2].rearrange("d (u s) -> d u s", s=P)
                copy(emb[:, :, :, NGATHER + k], source).then_inc(looked_taken, 1)
                coming = [j for j in range(NLOOK) if j % ID_SLOTS == k % ID_SLOTS and j > k][:1]
                if coming:
                    load_ids(turn, coming[0])
                elif not last:
                    load_ids(turn + 1, k % ID_SLOTS)

            def copy_groups(turn, u, groups=range(NG)):
                for g in groups:
                    if is_even(u, g):
                        copy_group(act, copy, turn, u, g, emb_act)

            def relu1(half, blocks=range(N1)):
                for n in blocks:
                    act.wait_ge(h1_full, half * N1 + (n // 2 * 2 + 2))
                    act.activation(h1_nb[:, n, :], h1_ps[:, n, :], ACT.Relu,
                                   bias=b1_sb[:, n:n + 1]).then_inc(h1_ready, 1)

            def relu2(half):
                for n in range(N2):
                    act.wait_ge(h2_full, half * N2 + (n // 2 * 2 + 2))
                    act.activation(h2[:, n, :], h2_ps[:, n, :], ACT.Relu,
                                   bias=b2_sb[:, n:n + 1]).then_inc(h2_ready, 1)

            def copy_y(turn, parity):
                act.wait_ge(y_full, turn * 2 + (parity + 1))
                if count(turn + parity):
                    act.wait_ge(y_stored[1 - parity], (turn + parity) * DMA)
                act.activation(y_sb, y_ps[parity], ACT.Copy).then_inc(y_ready, 1)

            for k, (_, table) in enumerate(looked):
                if k < ID_SLOTS:
                    load_ids(0, k)
                for first, end in ((0, TABLE_P // DMA * DMA), (TABLE_P // DMA * DMA, TABLE_P)):
                    act.dma_start(raw[k][first:end, :],
                                  table.rearrange("(p c) d -> p (c d)", c=chunks[k])[first:end, :]) \
                        .then_inc(table_in[k], DMA)
            for k in range(NLOOK):
                act.wait_ge(table_in[k], 2 * DMA)
                copy(table_hi[:, columns_of[k]], raw[k]).then_inc(hi_ready, 1)

            def handle(turn, last=False):
                take_looked_up(turn, 0, last)
                copy_groups(turn, 0)
                for k in range(1, NLOOK):
                    take_looked_up(turn, k, last)
                copy_groups(turn, 1, range(0, 2))
                copy_dots(act, copy, turn, 0, 0, dots_act)
                if count(turn):
                    relu1(turn * 2 - 2, range(0, 2))
                copy_groups(turn, 1, range(2, NG))
                if count(turn):
                    relu1(turn * 2 - 2, range(2, N1))
                copy_groups(turn, 2, range(0, 3))
                copy_dots(act, copy, turn, 1, 0, dots_act)
                if count(turn):
                    relu2(turn * 2 - 2)
                copy_groups(turn, 2, range(3, NG))
                if count(turn):
                    copy_y(turn - 1, 0)
                copy_groups(turn, 3, range(0, 2))
                copy_dots(act, copy, turn, 2, 0, dots_act)
                if count(turn):
                    relu1(turn * 2 - 1, range(0, 2))
                copy_groups(turn, 3, range(2, NG))
                if count(turn):
                    relu1(turn * 2 - 1, range(2, N1))
                copy_dots(act, copy, turn, 3, 0, dots_act)
                if count(turn):
                    relu2(turn * 2 - 1)
                    copy_y(turn - 1, 1)
                else:
                    act.wait_ge(weights_in, WEIGHTS)

            handle(0)
            with act.Fori(1, TURNS - 1) as turn:
                handle(turn)
            handle(TURNS - 1, last=True)
            relu1(TURNS * 2 - 2)
            relu2(TURNS * 2 - 2)
            copy_y(TURNS - 1, 0)
            relu1(TURNS * 2 - 1)
            relu2(TURNS * 2 - 1)
            copy_y(TURNS - 1, 1)

        @block.vector
        def _(dve):
            def copy(target, source):
                return dve.tensor_copy(target, source)

            def make_onehots(turn, k, part=None):
                part = range(chunks[k]) if part is None else part
                if part[0] == 0:
                    slot = k % ID_SLOTS
                    in_slot = len(range(slot, NLOOK, ID_SLOTS))
                    dve.wait_ge(ids_in[slot], turn * (in_slot * DMA) + (k // ID_SLOTS + 1) * DMA)
                for c in part:
                    n = before_feature[k] + c
                    if not count(turn) and c == 0:
                        dve.wait_ge(hi_ready, k + 1)
                        dve.tensor_tensor(table_lo[:, columns_of[k]], raw[k], table_hi[:, columns_of[k]].bitcast(F32),
                                          ALU.subtract).then_inc(lo_ready, 1)
                    if c >= ONEHOT_SLOTS:
                        used = n + 1 - ONEHOT_SLOTS
                    else:
                        size = chunks[k - 1]
                        used = before_feature[k] - size + max(j for j in range(size) if j % ONEHOT_SLOTS == c) + 1
                    if count(turn * ONEHOTS + used):
                        dve.wait_ge(onehot_used, turn * ONEHOTS + used)
                    dve.tensor_scalar(onehot[:, c % ONEHOT_SLOTS, :], ids_sb[0:TABLE_P, k % ID_SLOTS, :],
                                      row_ofs[chunks[k]][0:TABLE_P, c:c + 1], None, ALU.is_equal) \
                        .then_inc(onehot_ready, 1)

            def copy_x(turn, u):
                dve.wait_ge(x_in[u // 2], turn * DMA + DMA)
                if count(turn):
                    dve.wait_ge(dots_full[1], tiles_before(turn - 1, u) + 1)
                copy(emb[:, u, :, F], x_sb[:, u // 2, (u % 2) * P:(u % 2 + 1) * P]).then_inc(emb_x, 1)

            def copy_groups(turn, u, groups=range(NG)):
                for g in groups:
                    if not is_even(u, g):
                        copy_group(dve, copy, turn, u, g, emb_dve)

            def copy_idx(turn, u):
                copy(idx[:, u, :], idx_all[:, tiles_before(turn, u), :]).then_inc(idx_ready, 1)

            def copy_groups_and_make_onehots(turn, u, k):
                for g in range(NG):
                    copy_groups(turn, u, [g])
                    if g in (1, 2):
                        make_onehots(turn, k, range(2 * g + 2, 2 * g + 4))

            AHEAD, REST = range(ONEHOT_SLOTS), range(ONEHOT_SLOTS, chunks[0])

            def handle(turn, last=False):
                copy_groups_and_make_onehots(turn, 0, 1)
                for u in range(3 if count(turn) else 0, TILES_PER_TURN):
                    copy_x(turn, u)
                for k in range(2, NLOOK):
                    make_onehots(turn, k)
                for u in range(1, TILES_PER_TURN):
                    if u == 3 and not last:
                        make_onehots(turn + 1, 0, AHEAD)
                        copy_groups(turn, u, range(0, 4))
                        make_onehots(turn + 1, 0, REST)
                        copy_groups(turn, u, range(4, NG))
                    else:
                        copy_groups(turn, u)
                    copy_dots(dve, copy, turn, u - 1, 1, dots_dve)
                    if not last:
                        copy_idx(turn + 1, u - 1)
                if not last:
                    copy_idx(turn + 1, TILES_PER_TURN - 1)
                    make_onehots(turn + 1, 1, AHEAD)
                    for u in range(3):
                        copy_x(turn + 1, u)
                copy_dots(dve, copy, turn, 3, 1, dots_dve)

            dve.wait_ge(row_of_ready, len(sizes))
            dve.wait_ge(idx_in, DMA)
            make_onehots(0, 0)
            make_onehots(0, 1, AHEAD)
            handle(0)
            with dve.Fori(1, TURNS - 1) as turn:
                handle(turn)
            handle(TURNS - 1, last=True)


def kernel(**inputs):
    import numpy as np
    import concourse.bacc as bacc
    from concourse.bass_utils import run_bass_kernel_spmd

    ids = np.asarray(inputs["ids"])
    n_samples, n_tables = ids.shape
    names = [f"tbl_{f}" for f in range(n_tables)]
    arrays = {name: np.ascontiguousarray(inputs[name]) for name in names + ["ids", "W_top2"]}
    gathered, looked_up = features_by_way([arrays[name].shape[0] for name in names])
    order = gathered + looked_up + [n_tables]
    row = {pair: n for n, pair in enumerate(zip(*np.triu_indices(n_tables + 1, k=1)))}
    blocks, used = pair_blocks(n_tables + 1, P)
    w_top1 = np.asarray(inputs["W_top1"])
    w1 = np.zeros(((len(used) + 1) * P, w_top1.shape[1]), w_top1.dtype)
    for i, n, j, m, chunk, first in blocks:
        for a in range(n):
            for b in range(m):
                if i + a < j + b:
                    pair = order[i + a], order[j + b]
                    w1[chunk * P + first + a * m + b] = w_top1[row[min(pair), max(pair)]]
    w1[len(used) * P:] = w_top1[len(row):]
    arrays["w1"] = w1
    arrays["ids_looked"] = np.ascontiguousarray(ids.T[np.array(looked_up)])
    arrays["x_t"] = np.ascontiguousarray(np.asarray(inputs["r_dense_x"]).T)
    arrays["b1"] = np.ascontiguousarray(np.asarray(inputs["b_top1"]).reshape(-1, P).T)
    arrays["b2"] = np.ascontiguousarray(np.asarray(inputs["b_top2"]).reshape(-1, P).T)
    arrays["w3"] = np.ascontiguousarray(np.asarray(inputs["W_top3"]).reshape(-1, P).T)
    arrays = {f"in_{name}": a for name, a in arrays.items()}

    nc = bacc.Bacc("TRN2", target_bir_lowering=False, num_devices=1)
    d = {name: nc.dram_tensor(name, a.shape, mybir.dt.from_np(a.dtype), kind="ExternalInput").ap()
         for name, a in arrays.items()}
    y = nc.dram_tensor("y", (1, n_samples), F32, kind="ExternalOutput").ap()
    dlrm_tower(nc, d["in_x_t"], d["in_ids"], d["in_ids_looked"], [(f, d[f"in_tbl_{f}"]) for f in gathered],
               [(f, d[f"in_tbl_{f}"]) for f in looked_up], d["in_w1"], d["in_b1"], d["in_W_top2"], d["in_b2"],
               d["in_w3"], y)
    r = run_bass_kernel_spmd(nc, [arrays], core_ids=[0])
    return np.asarray(r.results[0]["y"]).reshape(n_samples, 1)
```
